# Optimizing a Trainium2 kernel written in Bass

```python
import numpy as np
import jax
import jax.numpy as jnp

def _softmax(x, axis=-1):
    return jax.nn.softmax(x, axis=axis)

def _gelu(x):
    return jax.nn.gelu(x, approximate=True)

def _silu(x):
    return jax.nn.silu(x)

def _sigmoid(x):
    return jax.nn.sigmoid(x)

def _layernorm(x, axis=-1, eps=1e-05):
    m = jnp.mean(x, axis=axis, keepdims=True)
    v = jnp.var(x, axis=axis, keepdims=True)
    return (x - m) / jnp.sqrt(v + eps)

def _scatter_add(tgt, idx, src, axis=0):
    return tgt.at[idx].add(src)

def _segment_sum(src, seg, n):
    return jax.ops.segment_sum(src, seg, n)
kernel_name = 'mk_dlrm_tower_d1_rec_r8_3235a7'

def setup_inputs(seed: int=0):
    np.random.seed(seed)
    _w = jnp.asarray

    def _rec_inputs():
        import jax
        import jax.numpy as jnp
        _tk = jax.random.key(seed)
        ids = jnp.stack([jax.random.randint(jax.random.fold_in(_tk, 200 + f), (2048,), 0, v, jnp.int32) for f, v in enumerate([1250, 125000, 1000, 1000, 1250, 12500, 12500, 1000, 12500, 1000, 1000, 1000, 1250, 1250, 12500, 1250, 12500, 1250, 1000, 1250, 1250, 1000, 1000, 12500, 1250, 1000])], axis=1)
        tbl_0 = 0.05 * jax.random.normal(jax.random.fold_in(_tk, 500 + 0), (1250, 128), jnp.float32)
        tbl_1 = 0.05 * jax.random.normal(jax.random.fold_in(_tk, 500 + 1), (125000, 128), jnp.float32)
        tbl_2 = 0.05 * jax.random.normal(jax.random.fold_in(_tk, 500 + 2), (1000, 128), jnp.float32)
        tbl_3 = 0.05 * jax.random.normal(jax.random.fold_in(_tk, 500 + 3), (1000, 128), jnp.float32)
        tbl_4 = 0.05 * jax.random.normal(jax.random.fold_in(_tk, 500 + 4), (1250, 128), jnp.float32)
        tbl_5 = 0.05 * jax.random.normal(jax.random.fold_in(_tk, 500 + 5), (12500, 128), jnp.float32)
        tbl_6 = 0.05 * jax.random.normal(jax.random.fold_in(_tk, 500 + 6), (12500, 128), jnp.float32)
        tbl_7 = 0.05 * jax.random.normal(jax.random.fold_in(_tk, 500 + 7), (1000, 128), jnp.float32)
        tbl_8 = 0.05 * jax.random.normal(jax.random.fold_in(_tk, 500 + 8), (12500, 128), jnp.float32)
        tbl_9 = 0.05 * jax.random.normal(jax.random.fold_in(_tk, 500 + 9), (1000, 128), jnp.float32)
        tbl_10 = 0.05 * jax.random.normal(jax.random.fold_in(_tk, 500 + 10), (1000, 128), jnp.float32)
        tbl_11 = 0.05 * jax.random.normal(jax.random.fold_in(_tk, 500 + 11), (1000, 128), jnp.float32)
        tbl_12 = 0.05 * jax.random.normal(jax.random.fold_in(_tk, 500 + 12), (1250, 128), jnp.float32)
        tbl_13 = 0.05 * jax.random.normal(jax.random.fold_in(_tk, 500 + 13), (1250, 128), jnp.float32)
        tbl_14 = 0.05 * jax.random.normal(jax.random.fold_in(_tk, 500 + 14), (12500, 128), jnp.float32)
        tbl_15 = 0.05 * jax.random.normal(jax.random.fold_in(_tk, 500 + 15), (1250, 128), jnp.float32)
        tbl_16 = 0.05 * jax.random.normal(jax.random.fold_in(_tk, 500 + 16), (12500, 128), jnp.float32)
        tbl_17 = 0.05 * jax.random.normal(jax.random.fold_in(_tk, 500 + 17), (1250, 128), jnp.float32)
        tbl_18 = 0.05 * jax.random.normal(jax.random.fold_in(_tk, 500 + 18), (1000, 128), jnp.float32)
        tbl_19 = 0.05 * jax.random.normal(jax.random.fold_in(_tk, 500 + 19), (1250, 128), jnp.float32)
        tbl_20 = 0.05 * jax.random.normal(jax.random.fold_in(_tk, 500 + 20), (1250, 128), jnp.float32)
        tbl_21 = 0.05 * jax.random.normal(jax.random.fold_in(_tk, 500 + 21), (1000, 128), jnp.float32)
        tbl_22 = 0.05 * jax.random.normal(jax.random.fold_in(_tk, 500 + 22), (1000, 128), jnp.float32)
        tbl_23 = 0.05 * jax.random.normal(jax.random.fold_in(_tk, 500 + 23), (12500, 128), jnp.float32)
        tbl_24 = 0.05 * jax.random.normal(jax.random.fold_in(_tk, 500 + 24), (1250, 128), jnp.float32)
        tbl_25 = 0.05 * jax.random.normal(jax.random.fold_in(_tk, 500 + 25), (1000, 128), jnp.float32)
        _rk = jax.random.fold_in(_tk, 7)
        r_dense_x = -0.000514642 + 1.00011 * jax.random.normal(jax.random.fold_in(_rk, 101), (2048, 128), jnp.float32)
        W_top1 = 0.0456912 * jax.random.normal(jax.random.fold_in(_tk, 801), (479, 512), jnp.float32)
        W_top2 = 0.0441942 * jax.random.normal(jax.random.fold_in(_tk, 802), (512, 256), jnp.float32)
        W_top3 = 0.0625 * jax.random.normal(jax.random.fold_in(_tk, 803), (256, 1), jnp.float32)
        b_top1 = jnp.zeros((512,), jnp.float32)
        b_top2 = jnp.zeros((256,), jnp.float32)
        return (r_dense_x, ids, tbl_0, tbl_1, tbl_2, tbl_3, tbl_4, tbl_5, tbl_6, tbl_7, tbl_8, tbl_9, tbl_10, tbl_11, tbl_12, tbl_13, tbl_14, tbl_15, tbl_16, tbl_17, tbl_18, tbl_19, tbl_20, tbl_21, tbl_22, tbl_23, tbl_24, tbl_25, W_top1, b_top1, W_top2, b_top2, W_top3)
    r_dense_x, ids, tbl_0, tbl_1, tbl_2, tbl_3, tbl_4, tbl_5, tbl_6, tbl_7, tbl_8, tbl_9, tbl_10, tbl_11, tbl_12, tbl_13, tbl_14, tbl_15, tbl_16, tbl_17, tbl_18, tbl_19, tbl_20, tbl_21, tbl_22, tbl_23, tbl_24, tbl_25, W_top1, b_top1, W_top2, b_top2, W_top3 = _rec_inputs()

    def _L0_rec_setup():
        import jax, jax.numpy as jnp
        import numpy as np
        F = 26
        D = 128
        B = 2048
        _TRIU_I, _TRIU_J = np.triu_indices(F + 1, k=1)
        _TRIU_I = jnp.asarray(_TRIU_I)
        _TRIU_J = jnp.asarray(_TRIU_J)
        key = jax.random.key(seed)
        k1, k2 = jax.random.split(key)
        sparse_x = jax.random.normal(k1, (B, F, D), dtype=jnp.float32)
        dense_x = jax.random.normal(k2, (B, D), dtype=jnp.float32)
        return {'sparse_x': sparse_x, 'dense_x': dense_x}
    _L0_rec_all = _L0_rec_setup()
    _L0_rec_in = {k: v for k, v in _L0_rec_all.items() if k in ()}
    del _L0_rec_all
    return {'r_dense_x': r_dense_x, 'ids': ids, 'tbl_0': tbl_0, 'tbl_1': tbl_1, 'tbl_2': tbl_2, 'tbl_3': tbl_3, 'tbl_4': tbl_4, 'tbl_5': tbl_5, 'tbl_6': tbl_6, 'tbl_7': tbl_7, 'tbl_8': tbl_8, 'tbl_9': tbl_9, 'tbl_10': tbl_10, 'tbl_11': tbl_11, 'tbl_12': tbl_12, 'tbl_13': tbl_13, 'tbl_14': tbl_14, 'tbl_15': tbl_15, 'tbl_16': tbl_16, 'tbl_17': tbl_17, 'tbl_18': tbl_18, 'tbl_19': tbl_19, 'tbl_20': tbl_20, 'tbl_21': tbl_21, 'tbl_22': tbl_22, 'tbl_23': tbl_23, 'tbl_24': tbl_24, 'tbl_25': tbl_25, 'W_top1': W_top1, 'b_top1': b_top1, 'W_top2': W_top2, 'b_top2': b_top2, 'W_top3': W_top3}

def reference(r_dense_x, ids, tbl_0, tbl_1, tbl_2, tbl_3, tbl_4, tbl_5, tbl_6, tbl_7, tbl_8, tbl_9, tbl_10, tbl_11, tbl_12, tbl_13, tbl_14, tbl_15, tbl_16, tbl_17, tbl_18, tbl_19, tbl_20, tbl_21, tbl_22, tbl_23, tbl_24, tbl_25, W_top1, b_top1, W_top2, b_top2, W_top3):
    import jax
    import jax.numpy as jnp

    def _L0_rec_ref(sparse_x, dense_x):
        import jax, jax.numpy as jnp
        import numpy as np
        F = 26
        D = 128
        B = 2048
        _TRIU_I, _TRIU_J = np.triu_indices(F + 1, k=1)
        _TRIU_I = jnp.asarray(_TRIU_I)
        _TRIU_J = jnp.asarray(_TRIU_J)
        combined = jnp.concatenate([sparse_x, dense_x[:, None, :]], axis=1)
        interact = jnp.einsum('bfd,bgd->bfg', combined, combined)
        return interact[:, _TRIU_I, _TRIU_J]
    e = jnp.stack([tbl_0[ids[:, 0]], tbl_1[ids[:, 1]], tbl_2[ids[:, 2]], tbl_3[ids[:, 3]], tbl_4[ids[:, 4]], tbl_5[ids[:, 5]], tbl_6[ids[:, 6]], tbl_7[ids[:, 7]], tbl_8[ids[:, 8]], tbl_9[ids[:, 9]], tbl_10[ids[:, 10]], tbl_11[ids[:, 11]], tbl_12[ids[:, 12]], tbl_13[ids[:, 13]], tbl_14[ids[:, 14]], tbl_15[ids[:, 15]], tbl_16[ids[:, 16]], tbl_17[ids[:, 17]], tbl_18[ids[:, 18]], tbl_19[ids[:, 19]], tbl_20[ids[:, 20]], tbl_21[ids[:, 21]], tbl_22[ids[:, 22]], tbl_23[ids[:, 23]], tbl_24[ids[:, 24]], tbl_25[ids[:, 25]]], axis=1)
    z = _L0_rec_ref(e, r_dense_x)
    z = z.reshape(z.shape[0], -1)
    h = jnp.concatenate([z, r_dense_x], axis=1)
    h = jnp.maximum(h @ W_top1 + b_top1, 0.0)
    h = jnp.maximum(h @ W_top2 + b_top2, 0.0)
    y = h @ W_top3
    return y

_drawn_inputs = setup_inputs


def setup_inputs(seed=0):
    import zlib

    import numpy as np

    out = dict(_drawn_inputs(seed))
    spreads = {'b_top1': (0.0, 0.1), 'b_top2': (0.0, 0.1)}
    factors = {}
    for name, (base, spread) in spreads.items():
        noise = np.random.default_rng([zlib.crc32(name.encode()), seed]).standard_normal(out[name].shape)
        drawn = base * np.exp(spread * noise) if base else spread * noise
        out[name] = jnp.asarray(drawn.astype(out[name].dtype))
    for name, factor in factors.items():
        out[name] = (out[name] * factor).astype(out[name].dtype)
    return out
```

```python
from contextlib import ExitStack

import numpy as np
import concourse.bass as bass
from concourse import mybir

F32 = mybir.dt.float32
I32 = mybir.dt.int32
ALU = mybir.AluOpType
ACT = mybir.ActivationFunctionType

P = 128
FIELDS = 26
VECS = FIELDS + 1
SLOT = 32
PER_MM = P // SLOT
QS = P // PER_MM
TILES_PER_CHUNK = 2
FGROUP = 4
GROUPS = [list(range(f, min(f + FGROUP, VECS))) for f in range(0, VECS, FGROUP)]
BANK = 512
PAIRS = FIELDS * VECS // 2
OFFSET = [f * FIELDS - f * (f - 1) // 2 for f in range(FIELDS)]
GRAM_Q = 8


def dlrm_tower(nc, x, ids, tables, w1, b1, w2, b2, w3, y):
    B, D = x.shape
    T = B // P
    CHUNKS = T // TILES_PER_CHUNK
    H1, H2 = w1.shape[1], w2.shape[1]
    M1, M2 = H1 // P, H2 // P
    NCOL = TILES_PER_CHUNK * P
    SQ = TILES_PER_CHUNK * QS
    PAIR_CHUNKS = [(c, min(P, PAIRS - c)) for c in range(0, PAIRS, P)]
    K1 = len(PAIR_CHUNKS) + 1

    x_v = x.rearrange("(p t) d -> p t d", t=T)
    ids_v = ids.rearrange("(p t) f -> p t f", t=T)
    y_v = y.rearrange("(p t) o -> p (t o)", t=T)

    with ExitStack() as ctx:
        def sb(name, shape, dt=F32):
            return ctx.enter_context(nc.sbuf_tensor(name, shape, dt))

        def ps(name, shape):
            return ctx.enter_context(nc.psum_tensor(name, shape, F32))

        def sem(name):
            return ctx.enter_context(nc.semaphore(name))

        idx = [sb(f"idx{s}", [P, FIELDS], I32) for s in range(2)]
        rows = [sb(f"rows{s}", [P, VECS, D]) for s in range(2)]
        vecs = [sb(f"vecs{s}", [P, QS, PER_MM, SLOT]) for s in range(2)]
        gram = sb("gram", [P, FIELDS, TILES_PER_CHUNK, QS])
        inter = sb("inter", [SQ, PER_MM, PAIRS])
        pairsT = sb("pairsT", [P, len(PAIR_CHUNKS), NCOL])
        denseT = sb("denseT", [P, NCOL])
        hid1 = sb("hid1", [P, M1, NCOL])
        hid2 = sb("hid2", [P, M2, NCOL])
        w1_sb = sb("w1_sb", [P, K1, H1])
        w2_sb = sb("w2_sb", [P, M1, H2])
        w3_sb = sb("w3_sb", [P, M2])
        b1_sb = sb("b1_sb", [P, M1])
        b2_sb = sb("b2_sb", [P, M2])
        y_sb = sb("y_sb", [P, T])
        ident = sb("ident", [P, P])

        tr_ps = [ps(f"tr_ps{b}", [P, FGROUP, P]) for b in range(2)]
        gram_ps = [ps(f"gram_ps{b}", [P, 2, BANK]) for b in range(2)]
        tower_ps = [ps(f"tower_ps{b}", [P, BANK]) for b in range(2)]

        weights_loaded = sem("weights_loaded")
        idx_loaded = [sem(f"idx_loaded{s}") for s in range(2)]
        rows_loaded = [[sem(f"rows_loaded{s}_{g}") for g in range(len(GROUPS))] for s in range(2)]
        dense_loaded = [sem(f"dense_loaded{s}") for s in range(2)]
        rows_free = [sem(f"rows_free{s}") for s in range(2)]
        ident_zeroed = sem("ident_zeroed")
        ident_ready = sem("ident_ready")
        pads_ready = sem("pads_ready")
        tr_ready = sem("tr_ready")
        tr_evac = [sem(f"tr_evac{b}") for b in range(2)]
        gram_ready = sem("gram_ready")
        gram_evac = [sem(f"gram_evac{b}") for b in range(2)]
        tower_ready = sem("tower_ready")
        tower_evac = [sem(f"tower_evac{b}") for b in range(2)]
        y_stored = sem("y_stored")
        pool_gate = sem("pool_gate")
        pe_gate = sem("pe_gate")

        NG = len(GROUPS)
        TRS = TILES_PER_CHUNK * NG
        TR_USES = TRS // 2
        GR = QS // GRAM_Q
        GRS = TILES_PER_CHUNK * GR
        ZGROUPS = [list(range(f, min(f + FGROUP, FIELDS))) for f in range(0, FIELDS, FGROUP)]
        N_Z = len(ZGROUPS)
        N_P = len(PAIR_CHUNKS)
        AT_P = N_Z
        AT_1 = AT_P + N_P
        AT_2 = AT_1 + M1
        AT_3 = AT_2 + M2
        USES = AT_3 + TILES_PER_CHUNK
        assert USES % 2 == 0 and TRS % 2 == 0 and GRS % 2 == 0

        block = ctx.enter_context(nc.Block())

        @block.sync
        def _(sp):
            with sp.Fori(0, CHUNKS) as i:
                for s in range(TILES_PER_CHUNK):
                    sp.wait_ge(rows_free[s], i + 1)
                    sp.dma_start(idx[s][:], ids_v[:, bass.ds(i * TILES_PER_CHUNK + s, 1), :]
                                 .rearrange("p a f -> p (a f)")).then_inc(idx_loaded[s], 16)
                    sp.dma_start(rows[s][:, FIELDS, :], x_v[:, bass.ds(i * TILES_PER_CHUNK + s, 1), :]
                                 .rearrange("p a d -> p (a d)")).then_inc(dense_loaded[s], 16)
            for b in range(2):
                sp.wait_ge(tower_evac[b], CHUNKS * USES // 2 + 1)
            sp.dma_start(y_v, y_sb[:]).then_inc(y_stored, 16)
            sp.wait_ge(y_stored, 16)

        @block.gpsimd
        def _(pool):
            pool.memset(ident[:], 0.0).then_inc(ident_zeroed, 1)
            pool.wait_ge(ident_zeroed, 1)
            pool.affine_select(out=ident[:], in_=ident[:], compare_op=ALU.not_equal, fill=1.0, base=0,
                               pattern=[[-1, P]], channel_multiplier=1).then_inc(ident_ready, 1)
            for s in range(2):
                pool.memset(vecs[s][:], 0.0).then_inc(pads_ready, 1)
            with pool.Fori(0, CHUNKS) as i:
                for s in range(TILES_PER_CHUNK):
                    pool.wait_ge(rows_free[s], i + 1)
                    pool.wait_ge(idx_loaded[s], 16 * i + 16)
                    pool.sem_inc(pool_gate)
                    for g, group in enumerate(GROUPS):
                        for f in group:
                            if f < FIELDS:
                                pool.indirect_dma_start(
                                    out=rows[s][:, f, :], out_offset=None, in_=tables[f][:, :],
                                    in_offset=bass.IndirectOffsetOnAxis(ap=idx[s][:, f:f + 1], axis=0),
                                ).then_inc(rows_loaded[s][g], 16)

        @block.tensor
        def _(pe):
            for s in range(2):
                pe.sem_inc(rows_free[s])
            pe.wait_ge(ident_ready, 1)
            pe.wait_ge(weights_loaded, 16 * 7)
            with pe.Fori(0, CHUNKS) as i:
                for s in range(TILES_PER_CHUNK):
                    for g, group in enumerate(GROUPS):
                        n = s * NG + g
                        pe.wait_ge(rows_loaded[s][g], 16 * len([f for f in group if f < FIELDS]) * (i + 1))
                        if group[-1] == FIELDS:
                            pe.wait_ge(dense_loaded[s], 16 * (i + 1))
                        pe.wait_ge(tr_evac[n % 2], TR_USES * i + n // 2 + 1)
                        for k, f in enumerate(group):
                            last = nc.tensor.transpose(tr_ps[n % 2][:, k, :], rows[s][:, f, :], ident[:])
                        last.then_inc(tr_ready, 1)
                    for b in range(2):
                        pe.wait_ge(tr_evac[b], TR_USES * i + ((s + 1) * NG + 1 - b) // 2 + 1)
                    for r in range(GR):
                        n = s * GR + r
                        pe.wait_ge(gram_evac[n % 2], 2 * (GRS // 2 * i + n // 2 + 1))
                        for k in range(GRAM_Q):
                            q = r * GRAM_Q + k
                            o = gram_ps[n % 2][:, k // 4, (k % 4) * PER_MM * FIELDS:(k % 4 + 1) * PER_MM * FIELDS]
                            last = nc.tensor.matmul(o, vecs[s][:, q, :, :].rearrange("p j f -> p (j f)"),
                                                    vecs[s][:, q, :, 0:FIELDS], start=True, stop=True)
                            if q == 0:
                                last.then_inc(rows_free[s], 1)
                        last.then_inc(gram_ready, 1)
                for b in range(2):
                    pe.wait_ge(gram_evac[b], 2 * (GRS // 2 * (i + 1) + 1))

                def bank(n):
                    pe.wait_ge(tower_evac[n % 2], USES // 2 * i + n // 2 + 1)
                    return tower_ps[n % 2]

                def before(n):
                    for b in range(2):
                        pe.wait_ge(tower_evac[b], USES // 2 * i + (n + 1 - b) // 2 + 1)

                for n, group in enumerate(ZGROUPS):
                    o = bank(n)
                    pe.sem_inc(pe_gate)
                    for k, f in enumerate(group):
                        last = nc.tensor.transpose(o[0:SQ, k * P:(k + 1) * P],
                                                   gram[:, f, :, :].rearrange("p s q -> p (s q)"), ident[:])
                    last.then_inc(tower_ready, 1)
                before(AT_P)
                for c, (at, size) in enumerate(PAIR_CHUNKS):
                    o = bank(AT_P + c)
                    pe.sem_inc(pe_gate)
                    for j in range(PER_MM):
                        last = nc.tensor.transpose(o[0:size, j * SQ:(j + 1) * SQ], inter[:, j, at:at + size],
                                                   ident[0:SQ, 0:SQ])
                    last.then_inc(tower_ready, 1)
                before(AT_1)
                for m in range(M1):
                    o = bank(AT_1 + m)
                    for c, (at, size) in enumerate(PAIR_CHUNKS):
                        nc.tensor.matmul(o[:, 0:NCOL], w1_sb[0:size, c, m * P:(m + 1) * P], pairsT[0:size, c, :],
                                         start=c == 0, stop=False)
                    nc.tensor.matmul(o[:, 0:NCOL], w1_sb[:, K1 - 1, m * P:(m + 1) * P],
                                     denseT[:],
                                     start=False, stop=True).then_inc(tower_ready, 1)
                before(AT_2)
                for m in range(M2):
                    o = bank(AT_2 + m)
                    for c in range(M1):
                        last = nc.tensor.matmul(o[:, 0:NCOL], w2_sb[:, c, m * P:(m + 1) * P], hid1[:, c, :],
                                                start=c == 0, stop=c == M1 - 1)
                    last.then_inc(tower_ready, 1)
                before(AT_3)
                for s in range(TILES_PER_CHUNK):
                    o = bank(AT_3 + s)
                    for c in range(M2):
                        last = nc.tensor.matmul(o[:, 0:1], hid2[:, c, s * P:(s + 1) * P], w3_sb[:, c:c + 1],
                                                start=c == 0, stop=c == M2 - 1)
                    last.then_inc(tower_ready, 1)

        def evacuate(eng, copy, relu, mine, i):
            def tr(n):
                s, g = divmod(n, NG)
                group = GROUPS[g]
                eng.wait_ge(tr_ready, TRS * i + n + 1)
                out = vecs[s][:, :, :, group[0]:group[0] + len(group)].rearrange("p q j f -> p f j q")
                src = tr_ps[n % 2][:, 0:len(group), :].rearrange("p f (j q) -> p f j q", j=PER_MM)
                if group[-1] == FIELDS:
                    copy(denseT[:, s * P:(s + 1) * P], tr_ps[n % 2][:, len(group) - 1, :])
                copy(out, src).then_inc(tr_evac[n % 2], 1)

            for s in range(TILES_PER_CHUNK):
                for g in range(NG):
                    if (s * NG + g) % 2 == mine:
                        tr(s * NG + g)
                for r in range(GR):
                    n = s * GR + r
                    eng.wait_ge(gram_ready, GRS * i + n + 1)
                    for j in (2 * mine, 2 * mine + 1):
                        quad = slice(j * SLOT, (j + 1) * SLOT)
                        src = gram_ps[n % 2][quad, :, 0:4 * PER_MM * FIELDS].rearrange(
                            "p b (k j f) -> p b k j f", k=4, j=PER_MM)[:, :, :, j, :]
                        out = gram[quad, :, s, r * GRAM_Q:(r + 1) * GRAM_Q].rearrange(
                            "p f (b k) -> p b k f", b=2)
                        last = copy(out, src)
                    last.then_inc(gram_evac[n % 2], 1)
            for n in range(USES):
                if n % 2 != mine:
                    continue
                eng.wait_ge(tower_ready, USES * i + n + 1)
                o = tower_ps[n % 2]
                if n < AT_P:
                    for k, f in enumerate(ZGROUPS[n]):
                        src = o[0:SQ, k * P:(k + 1) * P].rearrange("p (j f) -> p j f", j=PER_MM)
                        last = copy(inter[:, :, OFFSET[f]:OFFSET[f] + FIELDS - f], src[:, :, f + 1:VECS])
                elif n < AT_1:
                    size = PAIR_CHUNKS[n - AT_P][1]
                    out = pairsT[0:size, n - AT_P, :].rearrange("p (s j q) -> p j s q", s=TILES_PER_CHUNK, j=PER_MM)
                    last = copy(out, o[0:size, 0:NCOL].rearrange("p (j s q) -> p j s q", j=PER_MM, s=TILES_PER_CHUNK))
                elif n < AT_2:
                    m = n - AT_1
                    last = relu(hid1[:, m, :], o[:, 0:NCOL], b1_sb[:, m:m + 1])
                elif n < AT_3:
                    m = n - AT_2
                    last = relu(hid2[:, m, :], o[:, 0:NCOL], b2_sb[:, m:m + 1])
                else:
                    last = copy(y_sb[:, bass.ds(i * TILES_PER_CHUNK + n - AT_3, 1)], o[:, 0:1])
                last.then_inc(tower_evac[n % 2], 1)

        @block.vector
        def _(dve):
            dve.wait_ge(weights_loaded, 16 * 7)
            dve.wait_ge(pads_ready, 2)

            def copy(o, a):
                return nc.vector.tensor_copy(o, a)

            def relu(o, a, bias):
                return nc.vector.tensor_scalar(o, a, bias, 0.0, ALU.add, ALU.max)

            for evac in (tr_evac[0], gram_evac[0], gram_evac[1], tower_evac[0]):
                dve.sem_inc(evac)
            with dve.Fori(0, CHUNKS) as i:
                evacuate(dve, copy, relu, 0, i)

        @block.scalar
        def _(act):
            full = PAIRS // P
            act.dma_start(w1_sb[:, 0:full, :], w1[0:full * P, :].rearrange("(c p) n -> p c n", p=P)).then_inc(weights_loaded, 16)
            act.dma_start(w1_sb[0:PAIRS - full * P, full, :], w1[full * P:PAIRS, :]).then_inc(weights_loaded, 16)
            act.dma_start(w1_sb[:, K1 - 1, :], w1[PAIRS:PAIRS + D, :]).then_inc(weights_loaded, 16)
            act.dma_start(w2_sb[:], w2.rearrange("(c p) n -> p c n", p=P)).then_inc(weights_loaded, 16)
            with nc.allow_non_contiguous_dma(reason="biases and W_top3 one value per partition"):
                act.dma_start(w3_sb[:], w3.rearrange("(c p) o -> p (c o)", p=P)).then_inc(weights_loaded, 16)
                act.dma_start(b1_sb[:], b1.rearrange("(c p) -> p c", p=P)).then_inc(weights_loaded, 16)
                act.dma_start(b2_sb[:], b2.rearrange("(c p) -> p c", p=P)).then_inc(weights_loaded, 16)
            act.wait_ge(weights_loaded, 16 * 7)
            act.wait_ge(pads_ready, 2)

            def copy(o, a):
                return nc.scalar.activation(o, a, ACT.Copy)

            def relu(o, a, bias):
                return nc.scalar.activation(o, a, ACT.Relu, bias=bias)

            for evac in (tr_evac[1], gram_evac[0], gram_evac[1], tower_evac[1]):
                act.sem_inc(evac)
            with act.Fori(0, CHUNKS) as i:
                evacuate(act, copy, relu, 1, i)


def kernel(**inputs):
    import numpy as _np
    import concourse.bacc as _bacc
    from concourse import mybir as _mybir
    from concourse.bass_utils import run_bass_kernel_spmd as _run

    nc = _bacc.Bacc("TRN2", target_bir_lowering=False, num_devices=1)
    arrays, aps = {}, {}
    for name, a in inputs.items():
        a = _np.ascontiguousarray(a)
        arrays[f"in_{name}"] = a
        aps[name] = nc.dram_tensor(f"in_{name}", a.shape, _mybir.dt.from_np(a.dtype), kind="ExternalInput").ap()
    y = nc.dram_tensor("out_y", (inputs["ids"].shape[0], 1), _mybir.dt.float32, kind="ExternalOutput").ap()
    dlrm_tower(nc, aps["r_dense_x"], aps["ids"], [aps[f"tbl_{f}"] for f in range(FIELDS)],
               aps["W_top1"], aps["b_top1"], aps["W_top2"], aps["b_top2"], aps["W_top3"], y)
    return _run(nc, [arrays], core_ids=[0]).results[0]["out_y"]
```

```python
from contextlib import ExitStack

import numpy as np
import concourse.bass as bass
from concourse import mybir

F32 = mybir.dt.float32
F32R = mybir.dt.float32r
I32 = mybir.dt.int32
ALU = mybir.AluOpType
ACT = mybir.ActivationFunctionType

P = 128
FIELDS = 26
VECS = FIELDS + 1
SLOT = 32
PER_MM = P // SLOT
QS = P // PER_MM
TILES_PER_CHUNK = 2
FGROUP = 4
LOOKED_UP = [2, 3, 7, 9, 10, 18]
GROUPS = [[0, 4, 8, 12], [1, 6, 11, 16], [5, 13, 21], [14, 20, 26], [15, 17, 19], [22, 23, 24, 25]]
GATHERED = [f for group in GROUPS for f in group if f < FIELDS]
assert sorted(GATHERED + LOOKED_UP) == list(range(FIELDS))
BANK = 512
PAIRS = FIELDS * VECS // 2
OFFSET = [f * FIELDS - f * (f - 1) // 2 for f in range(FIELDS)]
GRAM_Q = 8


def dlrm_tower(nc, x, ids, lookup_ids, tables, w1, b1, w2, b2, w3, y):
    B, D = x.shape
    T = B // P
    CHUNKS = T // TILES_PER_CHUNK
    H1, H2 = w1.shape[1], w2.shape[1]
    M1, M2 = H1 // P, H2 // P
    NCOL = TILES_PER_CHUNK * P
    SQ = TILES_PER_CHUNK * QS
    PAIR_CHUNKS = [(c, min(P, PAIRS - c)) for c in range(0, PAIRS, P)]
    K1 = len(PAIR_CHUNKS) + 1

    ROWS = tables[LOOKED_UP[0]].shape[0]
    KT = -(-ROWS // P)
    KP = ROWS // KT
    assert all(tables[f].shape[0] == ROWS == KT * KP for f in LOOKED_UP)
    NL = len(LOOKED_UP)
    ONEHOTS = NL // 2
    assert NL == 2 * ONEHOTS

    x_v = x.rearrange("(p t) d -> p t d", t=T)
    ids_v = ids.rearrange("(p t) f -> p t f", t=T)
    y_v = y.rearrange("(p t) o -> p (t o)", t=T)

    with ExitStack() as ctx:
        def sb(name, shape, dt=F32):
            return ctx.enter_context(nc.sbuf_tensor(name, shape, dt))

        def ps(name, shape):
            return ctx.enter_context(nc.psum_tensor(name, shape, F32))

        def sem(name):
            return ctx.enter_context(nc.semaphore(name))

        idx = [sb(f"idx{s}", [P, FIELDS], I32) for s in range(2)]
        rows = [sb(f"rows{s}", [P, len(GATHERED) + 1, D]) for s in range(2)]
        place = {f: n for n, f in enumerate(GATHERED + [FIELDS])}
        vecs = sb("vecs", [P, TILES_PER_CHUNK, QS, PER_MM, SLOT])
        table = [sb(f"table{b}", [KP, KT, D]) for b in range(2)]
        table_hi = sb("table_hi", [KP, NL, KT, D], F32R)
        table_lo = sb("table_lo", [KP, NL, KT, D], F32R)
        row_no_i = sb("row_no_i", [KP, KT], I32)
        row_no = sb("row_no", [KP, KT])
        ids_bc = [sb(f"ids_bc{h}", [KP, ONEHOTS, NCOL], I32) for h in range(2)]
        onehot = sb("onehot", [KP, ONEHOTS, KT, NCOL], F32R)
        gram = sb("gram", [P, FIELDS, TILES_PER_CHUNK, QS])
        inter = sb("inter", [SQ, PER_MM, PAIRS])
        pairsT = sb("pairsT", [P, len(PAIR_CHUNKS), NCOL])
        dense_next = sb("dense_next", [P, NCOL])
        denseT = sb("denseT", [P, NCOL])
        hid1 = sb("hid1", [P, M1, NCOL])
        hid2 = sb("hid2", [P, M2, NCOL])
        w1_sb = sb("w1_sb", [P, K1, H1])
        w2_sb = sb("w2_sb", [P, M1, H2])
        w3_sb = sb("w3_sb", [P, M2])
        b1_sb = sb("b1_sb", [P, M1])
        b2_sb = sb("b2_sb", [P, M2])
        y_sb = sb("y_sb", [P, T])
        ident = sb("ident", [P, P])

        tr_ps = [ps(f"tr_ps{b}", [P, FGROUP, P]) for b in range(2)]
        gram_ps = [ps(f"gram_ps{b}", [P, 2, BANK]) for b in range(2)]
        tower_ps = [ps(f"tower_ps{b}", [P, BANK]) for b in range(2)]

        weights_loaded = sem("weights_loaded")
        table_loaded = [sem(f"table_loaded{b}") for b in range(2)]
        table_hi_done = sem("table_hi_done")
        table_split = sem("table_split")
        row_no_done = sem("row_no_done")
        row_no_ready = sem("row_no_ready")
        ids_bc_loaded = [sem(f"ids_bc_loaded{h}") for h in range(2)]
        onehot_ready = [sem(f"onehot_ready{n}") for n in range(ONEHOTS)]
        idx_loaded = [sem(f"idx_loaded{s}") for s in range(2)]
        rows_loaded = [[sem(f"rows_loaded{s}_{g}") for g in range(len(GROUPS))] for s in range(2)]
        dense_loaded = [sem(f"dense_loaded{s}") for s in range(2)]
        rows_free = [sem(f"rows_free{s}") for s in range(2)]
        ident_zeroed = sem("ident_zeroed")
        ident_ready = sem("ident_ready")
        pads_ready = sem("pads_ready")
        dense_ready = sem("dense_ready")
        tr_ready = sem("tr_ready")
        tr_evac = [sem(f"tr_evac{b}") for b in range(2)]
        gram_ready = sem("gram_ready")
        gram_evac = [sem(f"gram_evac{b}") for b in range(2)]
        tower_ready = sem("tower_ready")
        tower_evac = [sem(f"tower_evac{b}") for b in range(2)]
        y_stored = sem("y_stored")
        pool_gate = sem("pool_gate")
        pe_gate = sem("pe_gate")

        NG = len(GROUPS)
        TRS = NL + TILES_PER_CHUNK * NG
        DENSE_USE = NL + [FIELDS in group for group in GROUPS].index(True)
        assert NG % 2 == 0
        TR_USES = TRS // 2
        GR = QS // GRAM_Q
        GRS = TILES_PER_CHUNK * GR
        ZGROUPS = [list(range(f, min(f + FGROUP, FIELDS))) for f in range(0, FIELDS, FGROUP)]
        N_Z = len(ZGROUPS)
        rows_of = lambda s: [("rows", s, g) for g in range(NG)]
        grams_of = lambda s: [("gram", s, r) for r in range(GR)]
        samples = [("samples", n) for n in range(N_Z)]
        pairs = [("pairs", c) for c in range(len(PAIR_CHUNKS))]
        layer1s, layer2s = [("layer1", m) for m in range(M1)], [("layer2", m) for m in range(M2)]
        layer3s = [("layer3", s) for s in range(TILES_PER_CHUNK)]

        def between(a, b):
            out, used = [], 0
            for n, step in enumerate(a):
                out.append(step)
                until = len(b) * (n + 1) // len(a)
                out += b[used:until]
                used = until
            return out

        TOWER = samples + pairs + layer1s + layer2s + layer3s
        ROUND = (between(rows_of(0), samples) + between(grams_of(0), pairs) + between(rows_of(1), layer1s)
                 + between(grams_of(1), layer2s + layer3s))
        N_P = len(PAIR_CHUNKS)
        AT_P = N_Z
        AT_1 = AT_P + N_P
        AT_2 = AT_1 + M1
        AT_3 = AT_2 + M2
        USES = AT_3 + TILES_PER_CHUNK
        assert USES % 2 == 0 and TRS % 2 == 0 and GRS % 2 == 0

        def lookup_out(n):
            return tr_ps[n % 2][:, 0:TILES_PER_CHUNK, :]

        block = ctx.enter_context(nc.Block())

        @block.sync
        def _(sp):
            def load_ids_bc(h, chunk):
                sp.dma_start(ids_bc[h][:], lookup_ids[h * ONEHOTS:(h + 1) * ONEHOTS, bass.ds(chunk * NCOL, NCOL)]
                             .unsqueeze(0).to_broadcast([KP, ONEHOTS, NCOL])).then_inc(ids_bc_loaded[h], 16)

            def load_tiles(i):
                for s in range(TILES_PER_CHUNK):
                    sp.wait_ge(rows_free[s], i + 1)
                    t = bass.ds(i * TILES_PER_CHUNK + s, 1)
                    sp.dma_start(idx[s][:], ids_v[:, t, :].rearrange("p a f -> p (a f)")).then_inc(idx_loaded[s], 16)
                    sp.dma_start(rows[s][:, place[FIELDS], :],
                                 x_v[:, t, :].rearrange("p a d -> p (a d)")).then_inc(dense_loaded[s], 16)

            load_tiles(0)
            for h in range(2):
                load_ids_bc(h, 0)
            for n, f in enumerate(LOOKED_UP):
                if n >= 2:
                    sp.wait_ge(table_split, n - 1)
                sp.dma_start(table[n % 2][:], tables[f].rearrange("(p k) d -> p k d", k=KT)).then_inc(
                    table_loaded[n % 2], 16)
            with sp.Fori(1, CHUNKS) as i:
                for h in range(2):
                    sp.wait_ge(onehot_ready[ONEHOTS - 1], 2 * i - 1 + h)
                    load_ids_bc(h, i)
                load_tiles(i)
            for b in range(2):
                sp.wait_ge(tower_evac[b], CHUNKS * USES // 2 + 1)
            sp.dma_start(y_v, y_sb[:]).then_inc(y_stored, 16)
            sp.wait_ge(y_stored, 16)

        @block.gpsimd
        def _(pool):
            pool.memset(ident[:], 0.0).then_inc(ident_zeroed, 1)
            pool.wait_ge(ident_zeroed, 1)
            pool.affine_select(out=ident[:], in_=ident[:], compare_op=ALU.not_equal, fill=1.0, base=0,
                               pattern=[[-1, P]], channel_multiplier=1).then_inc(ident_ready, 1)
            pool.iota(row_no_i[:], pattern=[[1, KT]], base=0, channel_multiplier=KT).then_inc(row_no_done, 1)
            for s in range(2):
                pool.memset(vecs[:, s, :, :, VECS:SLOT], 0.0).then_inc(pads_ready, 1)
            with pool.Fori(0, CHUNKS) as i:
                for s in range(TILES_PER_CHUNK):
                    pool.wait_ge(rows_free[s], i + 1)
                    pool.wait_ge(idx_loaded[s], 16 * i + 16)
                    pool.sem_inc(pool_gate)
                    for g, group in enumerate(GROUPS):
                        for f in group:
                            if f < FIELDS:
                                pool.indirect_dma_start(
                                    out=rows[s][:, place[f], :], out_offset=None, in_=tables[f][:, :],
                                    in_offset=bass.IndirectOffsetOnAxis(ap=idx[s][:, f:f + 1], axis=0),
                                ).then_inc(rows_loaded[s][g], 16)

        @block.tensor
        def _(pe):
            for s in range(2):
                pe.sem_inc(rows_free[s])
            pe.wait_ge(ident_ready, 1)

            def look_up(i):
                for n in range(NL):
                    pe.wait_ge(tr_evac[n % 2], TR_USES * i + n // 2 + 1)
                    pe.wait_ge(onehot_ready[n % ONEHOTS], 2 * i + n // ONEHOTS + 1)
                    products = [(part, k) for part in (table_hi, table_lo) for k in range(KT)]
                    for part, k in products:
                        last = nc.tensor.matmul(lookup_out(n), part[:, n, k, :], onehot[:, n % ONEHOTS, k, :],
                                                start=(part, k) == products[0], stop=(part, k) == products[-1])
                    last.then_inc(tr_ready, 1)

            def transpose_rows(i, s, g):
                group = GROUPS[g]
                n = NL + s * NG + g
                pe.wait_ge(rows_loaded[s][g], 16 * len([f for f in group if f < FIELDS]) * (i + 1))
                if FIELDS in group:
                    pe.wait_ge(dense_loaded[s], 16 * (i + 1))
                pe.wait_ge(tr_evac[n % 2], TR_USES * i + n // 2 + 1)
                for k, f in enumerate(group):
                    last = nc.tensor.transpose(tr_ps[n % 2][:, k, :], rows[s][:, place[f], :], ident[:])
                last.then_inc(tr_ready, 1)

            def gram_products(i, s, r):
                if r == 0:
                    for b in range(2):
                        pe.wait_ge(tr_evac[b], TR_USES * i + (NL + (s + 1) * NG + 1 - b) // 2 + 1)
                n = s * GR + r
                pe.wait_ge(gram_evac[n % 2], 2 * (GRS // 2 * i + n // 2 + 1))
                for k in range(GRAM_Q):
                    q = r * GRAM_Q + k
                    o = gram_ps[n % 2][:, k // 4, (k % 4) * PER_MM * FIELDS:(k % 4 + 1) * PER_MM * FIELDS]
                    last = nc.tensor.matmul(o, vecs[:, s, q, :, :].rearrange("p j f -> p (j f)"),
                                            vecs[:, s, q, :, 0:FIELDS], start=True, stop=True)
                    if q == 0:
                        last.then_inc(rows_free[s], 1)
                last.then_inc(gram_ready, 1)

            def tower_bank(i, n):
                pe.wait_ge(tower_evac[n % 2], USES // 2 * i + n // 2 + 1)
                return tower_ps[n % 2]

            def tower_evacuated(i, n):
                for b in range(2):
                    pe.wait_ge(tower_evac[b], USES // 2 * i + (n + 1 - b) // 2 + 1)

            def samples_up(i, n):
                if n == 0:
                    for b in range(2):
                        pe.wait_ge(gram_evac[b], 2 * (GRS // 2 * (i + 1) + 1))
                o = tower_bank(i, n)
                pe.sem_inc(pe_gate)
                for k, f in enumerate(ZGROUPS[n]):
                    last = nc.tensor.transpose(o[0:SQ, k * P:(k + 1) * P],
                                               gram[:, f, :, :].rearrange("p s q -> p (s q)"), ident[:])
                last.then_inc(tower_ready, 1)

            def pairs_up(i, c):
                if c == 0:
                    tower_evacuated(i, AT_P)
                at, size = PAIR_CHUNKS[c]
                o = tower_bank(i, AT_P + c)
                pe.sem_inc(pe_gate)
                for j in range(PER_MM):
                    last = nc.tensor.transpose(o[0:size, j * SQ:(j + 1) * SQ], inter[:, j, at:at + size],
                                               ident[0:SQ, 0:SQ])
                last.then_inc(tower_ready, 1)

            def layer1(i, m):
                if m == 0:
                    pe.wait_ge(dense_ready, i + 1)
                    tower_evacuated(i, AT_1)
                o = tower_bank(i, AT_1 + m)
                for c, (at, size) in enumerate(PAIR_CHUNKS):
                    nc.tensor.matmul(o[:, 0:NCOL], w1_sb[0:size, c, m * P:(m + 1) * P], pairsT[0:size, c, :],
                                     start=c == 0, stop=False)
                nc.tensor.matmul(o[:, 0:NCOL], w1_sb[:, K1 - 1, m * P:(m + 1) * P], denseT[:],
                                 start=False, stop=True).then_inc(tower_ready, 1)

            def layer2(i, m):
                if m == 0:
                    tower_evacuated(i, AT_2)
                o = tower_bank(i, AT_2 + m)
                for c in range(M1):
                    last = nc.tensor.matmul(o[:, 0:NCOL], w2_sb[:, c, m * P:(m + 1) * P], hid1[:, c, :],
                                            start=c == 0, stop=c == M1 - 1)
                last.then_inc(tower_ready, 1)

            def layer3(i, s):
                if s == 0:
                    tower_evacuated(i, AT_3)
                o = tower_bank(i, AT_3 + s)
                for c in range(M2):
                    last = nc.tensor.matmul(o[:, 0:1], hid2[:, c, s * P:(s + 1) * P], w3_sb[:, c:c + 1],
                                            start=c == 0, stop=c == M2 - 1)
                last.then_inc(tower_ready, 1)

            def chunk(i, first=False, last=False):
                if first:
                    pe.wait_ge(weights_loaded, 16 * 7)
                for stage, *at in ROUND:
                    if stage == "rows":
                        transpose_rows(i, *at)
                    elif stage == "gram":
                        gram_products(i, *at)
                    elif not first:
                        tower(i - 1, stage, *at)
                if not last:
                    look_up(i + 1)

            def tower(i, stage, n):
                {"samples": samples_up, "pairs": pairs_up, "layer1": layer1, "layer2": layer2,
                 "layer3": layer3}[stage](i, n)

            look_up(0)
            chunk(0, first=True)
            with pe.Fori(1, CHUNKS - 1) as i:
                chunk(i)
            chunk(CHUNKS - 1, last=True)
            for step in TOWER:
                tower(CHUNKS - 1, *step)

        def evacuate(eng, copy, relu, mine, quads, make_onehots=None):
            dense_mine = mine == DENSE_USE % 2

            def evac_lookups(i):
                for n in range(NL):
                    if n % 2 == mine:
                        eng.wait_ge(tr_ready, TRS * i + n + 1)
                        out = vecs[:, :, :, :, LOOKED_UP[n]].rearrange("p s q j -> p s j q")
                        src = lookup_out(n).rearrange("p s (j q) -> p s j q", j=PER_MM)
                        copy(out, src).then_inc(tr_evac[mine], 1)
                    if make_onehots and n < ONEHOTS:
                        eng.wait_ge(tr_ready, TRS * i + n + 1)
                        for k in range(KT):
                            make_onehots(i, 1, n, k)

            def evac_rows(i, s, g):
                group = GROUPS[g]
                n = NL + s * NG + g
                if n % 2 != mine:
                    return
                step = group[1] - group[0]
                eng.wait_ge(tr_ready, TRS * i + n + 1)
                out = vecs[:, s, :, :, group[0]:group[-1] + 1:step].rearrange("p q j f -> p f j q")
                src = tr_ps[mine][:, 0:len(group), :].rearrange("p f (j q) -> p f j q", j=PER_MM)
                if group[-1] == FIELDS:
                    copy(dense_next[:, s * P:(s + 1) * P], tr_ps[mine][:, len(group) - 1, :])
                copy(out, src).then_inc(tr_evac[mine], 1)

            def evac_gram(i, s, r):
                n = s * GR + r
                eng.wait_ge(gram_ready, GRS * i + n + 1)
                for j in quads:
                    quad = slice(j * SLOT, (j + 1) * SLOT)
                    src = gram_ps[n % 2][quad, :, 0:4 * PER_MM * FIELDS].rearrange(
                        "p b (k j f) -> p b k j f", k=4, j=PER_MM)[:, :, :, j, :]
                    out = gram[quad, :, s, r * GRAM_Q:(r + 1) * GRAM_Q].rearrange(
                        "p f (b k) -> p b k f", b=2)
                    last = copy(out, src)
                last.then_inc(gram_evac[n % 2], 1)

            def keep_dense(i):
                if dense_mine:
                    eng.wait_ge(tr_evac[mine], TR_USES * i + (NL + TILES_PER_CHUNK * NG + 1 - mine) // 2 + 1)
                    copy(denseT[:], dense_next[:]).then_inc(dense_ready, 1)
                    eng.wait_ge(dense_ready, i + 1)

            def evac_tower(i, stage, at):
                n = {"samples": 0, "pairs": AT_P, "layer1": AT_1, "layer2": AT_2, "layer3": AT_3}[stage] + at
                if n % 2 != mine:
                    return
                eng.wait_ge(tower_ready, USES * i + n + 1)
                o = tower_ps[mine]
                if stage == "samples":
                    for k, f in enumerate(ZGROUPS[at]):
                        src = o[0:SQ, k * P:(k + 1) * P].rearrange("p (j f) -> p j f", j=PER_MM)
                        last = copy(inter[:, :, OFFSET[f]:OFFSET[f] + FIELDS - f], src[:, :, f + 1:VECS])
                elif stage == "pairs":
                    size = PAIR_CHUNKS[at][1]
                    out = pairsT[0:size, at, :].rearrange("p (s j q) -> p j s q", s=TILES_PER_CHUNK, j=PER_MM)
                    last = copy(out, o[0:size, 0:NCOL].rearrange("p (j s q) -> p j s q", j=PER_MM,
                                                                 s=TILES_PER_CHUNK))
                elif stage == "layer1":
                    last = relu(hid1[:, at, :], o[:, 0:NCOL], b1_sb[:, at:at + 1])
                elif stage == "layer2":
                    last = relu(hid2[:, at, :], o[:, 0:NCOL], b2_sb[:, at:at + 1])
                else:
                    last = copy(y_sb[:, bass.ds(i * TILES_PER_CHUNK + at, 1)], o[:, 0:1])
                last.then_inc(tower_evac[mine], 1)

            def chunk(i, first=False, last=False):
                if first:
                    eng.wait_ge(weights_loaded, 16 * 7)
                else:
                    keep_dense(i - 1)
                made = 0
                for at_step, (stage, *at) in enumerate(ROUND):
                    if stage == "rows":
                        evac_rows(i, *at)
                    elif stage == "gram":
                        evac_gram(i, *at)
                    elif not first:
                        evac_tower(i - 1, stage, *at)
                    if make_onehots and not last and at_step >= NG:
                        until = ONEHOTS * KT * (at_step + 1 - NG) // (len(ROUND) - NG)
                        for step in range(made, until):
                            make_onehots(i + 1, 0, step // KT, step % KT)
                        made = until
                if not last:
                    evac_lookups(i + 1)

            for evac in (tr_evac[mine], gram_evac[0], gram_evac[1], tower_evac[mine]):
                eng.sem_inc(evac)
            evac_lookups(0)
            eng.wait_ge(pads_ready, 2)
            chunk(0, first=True)
            with eng.Fori(1, CHUNKS - 1) as i:
                chunk(i)
            chunk(CHUNKS - 1, last=True)
            keep_dense(CHUNKS - 1)
            for step in TOWER:
                evac_tower(CHUNKS - 1, *step)

        @block.vector
        def _(dve):
            def copy(o, a):
                return nc.vector.tensor_copy(o, a)

            def relu(o, a, bias):
                return nc.vector.tensor_scalar(o, a, bias, 0.0, ALU.add, ALU.max)

            dve.wait_ge(row_no_done, 1)
            nc.vector.tensor_copy(row_no[:], row_no_i[:]).then_inc(row_no_ready, 1)
            for n in range(NL):
                dve.wait_ge(table_loaded[n % 2], 16 * (n // 2 + 1))
                nc.vector.tensor_copy(table_hi[:, n], table[n % 2][:]).then_inc(table_hi_done, 1)
                dve.wait_ge(table_hi_done, n + 1)
                nc.vector.tensor_tensor(table_lo[:, n], table[n % 2][:], table_hi[:, n].bitcast(F32),
                                        ALU.subtract).then_inc(table_split, 1)
            dve.wait_ge(row_no_ready, 1)

            def make_onehots(i, h, o, k):
                if o == 0 and k == 0:
                    dve.wait_ge(ids_bc_loaded[h], 16 * (i + 1))
                made = nc.vector.tensor_scalar(onehot[:, o, k, :], ids_bc[h][:, o, :], row_no[:, k:k + 1], None,
                                               ALU.is_equal)
                if k == KT - 1:
                    made.then_inc(onehot_ready[o], 1)

            for o in range(ONEHOTS):
                for k in range(KT):
                    make_onehots(0, 0, o, k)
            evacuate(dve, copy, relu, 0, [0], make_onehots)

        @block.scalar
        def _(act):
            full = PAIRS // P
            act.dma_start(w1_sb[:, 0:full, :], w1[0:full * P, :].rearrange("(c p) n -> p c n", p=P)).then_inc(weights_loaded, 16)
            act.dma_start(w1_sb[0:PAIRS - full * P, full, :], w1[full * P:PAIRS, :]).then_inc(weights_loaded, 16)
            act.dma_start(w1_sb[:, K1 - 1, :], w1[PAIRS:PAIRS + D, :]).then_inc(weights_loaded, 16)
            act.dma_start(w2_sb[:], w2.rearrange("(c p) n -> p c n", p=P)).then_inc(weights_loaded, 16)
            with nc.allow_non_contiguous_dma(reason="biases and W_top3 one value per partition"):
                act.dma_start(w3_sb[:], w3.rearrange("(c p) o -> p (c o)", p=P)).then_inc(weights_loaded, 16)
                act.dma_start(b1_sb[:], b1.rearrange("(c p) -> p c", p=P)).then_inc(weights_loaded, 16)
                act.dma_start(b2_sb[:], b2.rearrange("(c p) -> p c", p=P)).then_inc(weights_loaded, 16)
            def copy(o, a):
                return nc.scalar.activation(o, a, ACT.Copy)

            def relu(o, a, bias):
                return nc.scalar.activation(o, a, ACT.Relu, bias=bias)

            evacuate(act, copy, relu, 1, [1, 2, 3])


def kernel(**inputs):
    import numpy as _np
    import concourse.bacc as _bacc
    from concourse import mybir as _mybir
    from concourse.bass_utils import run_bass_kernel_spmd as _run

    nc = _bacc.Bacc("TRN2", target_bir_lowering=False, num_devices=1)
    arrays, aps = {}, {}
    for name, a in inputs.items():
        a = _np.ascontiguousarray(a)
        arrays[f"in_{name}"] = a
        aps[name] = nc.dram_tensor(f"in_{name}", a.shape, _mybir.dt.from_np(a.dtype), kind="ExternalInput").ap()
    order = _np.ascontiguousarray(inputs["ids"]).reshape(P, -1, FIELDS)[:, :, LOOKED_UP].transpose(2, 1, 0)
    arrays["in_lookup_ids"] = _np.ascontiguousarray(order).reshape(len(LOOKED_UP), -1)
    lookup_ids = nc.dram_tensor("in_lookup_ids", arrays["in_lookup_ids"].shape, _mybir.dt.int32, kind="ExternalInput").ap()
    y = nc.dram_tensor("out_y", (inputs["ids"].shape[0], 1), _mybir.dt.float32, kind="ExternalOutput").ap()
    dlrm_tower(nc, aps["r_dense_x"], aps["ids"], lookup_ids, [aps[f"tbl_{f}"] for f in range(FIELDS)],
               aps["W_top1"], aps["b_top1"], aps["W_top2"], aps["b_top2"], aps["W_top3"], y)
    return _run(nc, [arrays], core_ids=[0]).results[0]["out_y"]
```

```python
from contextlib import ExitStack
from itertools import product

import concourse.bass as bass
from concourse import mybir

F32 = mybir.dt.float32
F32R = mybir.dt.float32r
I32 = mybir.dt.int32
ALU = mybir.AluOpType
ACT = mybir.ActivationFunctionType

P = 128
FIELDS = 26
VECS = FIELDS + 1
SLOT = 32
PER_MM = P // SLOT
QS = P // PER_MM
TILES_PER_CHUNK = 2
FGROUP = 4
LOOKED_UP = [2, 3, 7, 9, 10, 18]
GROUPS = [[0, 4, 8, 12], [1, 6, 11, 16], [13, 14, 15], [5, 17], [19, 20, 21], [22, 23, 24, 25]]
GATHERED = [f for group in GROUPS for f in group]
assert sorted(GATHERED + LOOKED_UP) == list(range(FIELDS))
BANK = 512
PAIRS = FIELDS * VECS // 2
RUNS = [[6, 7, 8, 9, 10, 12, 14, 16, 18, 20, 22, 24, 26], [1, 2, 3, 4, 5, 11, 13, 15, 17, 19, 21, 23, 25]]
RUN_PAIRS = [sum(run) for run in RUNS]
assert sorted(RUNS[0] + RUNS[1]) == list(range(1, VECS)) and all(P < n < 2 * P for n in RUN_PAIRS)
LEFT = RUN_PAIRS[1] - P
RUN_AT = [0, RUN_PAIRS[0] + max(LEFT, SLOT)]
INTER = RUN_AT[1] + RUN_PAIRS[1] - RUNS[1][-1] + SLOT
SAMPLE_STEPS = [(run[k], RUN_AT[n] + sum(run[:k])) for k in range(len(RUNS[0])) for n, run in enumerate(RUNS)]
ENDS = [1 + max(step for step, (f, at) in enumerate(SAMPLE_STEPS) if f in run and at < start + P)
        for run, start in zip(RUNS, RUN_AT)]
PAIR_STEPS = [(0, P, ENDS[0]), (RUN_AT[1], P, ENDS[1]), (P, PAIRS - 2 * P, FIELDS + 1)]
COPIED = FIELDS + 1
GRAM_M = P - SLOT + FIELDS
GRAM_Q = 8


def dlrm_tower(nc, x_cols, ids, lookup_ids, tables, w1, b1, w2, b2, w3, y):
    D, B = x_cols.shape
    T = B // P
    CHUNKS = T // TILES_PER_CHUNK
    H1, H2 = w1.shape[1], w2.shape[1]
    M1, M2 = H1 // P, H2 // P
    NCOL = TILES_PER_CHUNK * P
    N_P = len(PAIR_STEPS)

    ROWS = tables[LOOKED_UP[0]].shape[0]
    KT = -(-ROWS // P)
    KP = ROWS // KT
    assert all(tables[f].shape[0] == ROWS == KT * KP for f in LOOKED_UP)
    NL = len(LOOKED_UP)
    ONEHOTS = NL // 2
    assert NL == 2 * ONEHOTS

    x_v = x_cols.rearrange("d (t p) -> d t p", t=T)
    ids_v = ids.rearrange("(p t) f -> p t f", t=T)
    y_v = y.rearrange("(p t) o -> p (t o)", t=T)

    with ExitStack() as ctx:
        def sb(name, shape, dt=F32):
            return ctx.enter_context(nc.sbuf_tensor(name, shape, dt))

        def ps(name, shape):
            return ctx.enter_context(nc.psum_tensor(name, shape, F32))

        def sem(name):
            return ctx.enter_context(nc.semaphore(name))

        idx = [sb(f"idx{s}", [P, FIELDS], I32) for s in range(2)]
        rows = [sb(f"rows{s}", [P, len(GATHERED), D]) for s in range(2)]
        place = {f: n for n, f in enumerate(GATHERED)}
        vecs = sb("vecs", [P, TILES_PER_CHUNK, QS, PER_MM, SLOT])
        staged = [sb(f"staged{b}", [P, KT * D]) for b in range(2)]
        table_hi = sb("table_hi", [KP, NL, KT, D], F32R)
        table_lo = sb("table_lo", [KP, NL, KT, D], F32R)
        row_no_i = sb("row_no_i", [KP, KT], I32)
        row_no = sb("row_no", [KP, KT])
        ids_bc = [sb(f"ids_bc{h}", [KP, ONEHOTS, NCOL], I32) for h in range(2)]
        onehot = sb("onehot", [KP, ONEHOTS, KT, NCOL], F32R)
        gram = sb("gram", [P, FIELDS, TILES_PER_CHUNK, QS])
        inter = sb("inter", [P, TILES_PER_CHUNK, INTER])
        pairs_hi = sb("pairs_hi", [P, N_P, NCOL], F32R)
        pairs_lo = sb("pairs_lo", [P, N_P, NCOL], F32R)
        dense_next = sb("dense_next", [P, NCOL])
        dense_hi = sb("dense_hi", [P, NCOL], F32R)
        dense_lo = sb("dense_lo", [P, NCOL], F32R)
        hid1 = [sb(f"hid1_{b}", [P, NCOL]) for b in range(2)]
        hid1_hi = sb("hid1_hi", [P, M1, NCOL], F32R)
        hid1_lo = sb("hid1_lo", [P, M1, NCOL], F32R)
        hid2 = sb("hid2", [P, M2, NCOL])
        w1_hi = sb("w1_hi", [P, N_P + 1, H1], F32R)
        w1_lo = sb("w1_lo", [P, N_P + 1, H1], F32R)
        w2_hi = sb("w2_hi", [P, M1, H2], F32R)
        w2_lo = sb("w2_lo", [P, M1, H2], F32R)
        w3_sb = sb("w3_sb", [P, M2])
        b1_sb = sb("b1_sb", [P, M1])
        b2_sb = sb("b2_sb", [P, M2])
        y_sb = sb("y_sb", [P, T])
        ident = sb("ident", [P, P])

        tr_ps = [ps(f"tr_ps{b}", [P, FGROUP, P]) for b in range(2)]
        gram_ps = [ps(f"gram_ps{b}", [P, 2, BANK]) for b in range(2)]
        tower_ps = [ps(f"tower_ps{b}", [P, BANK]) for b in range(2)]

        weights_loaded = sem("weights_loaded")
        staged_loaded = [sem(f"staged_loaded{b}") for b in range(2)]
        staged_hi = sem("staged_hi")
        staged_split = sem("staged_split")
        hi_ready = sem("hi_ready")
        hid1_split = sem("hid1_split")
        row_no_done = sem("row_no_done")
        row_no_ready = sem("row_no_ready")
        ids_bc_loaded = [sem(f"ids_bc_loaded{h}") for h in range(2)]
        onehot_ready = [sem(f"onehot_ready{n}") for n in range(ONEHOTS)]
        idx_loaded = [sem(f"idx_loaded{s}") for s in range(2)]
        rows_loaded = [[sem(f"rows_loaded{s}_{g}") for g in range(len(GROUPS))] for s in range(2)]
        dense_loaded = sem("dense_loaded")
        ident_zeroed = sem("ident_zeroed")
        ident_ready = sem("ident_ready")
        pads_ready = sem("pads_ready")
        samples_up = [sem(f"samples_up{s}") for s in range(TILES_PER_CHUNK)]
        dense_ready = sem("dense_ready")
        tr_ready = sem("tr_ready")
        tr_evac = sem("tr_evac")
        gram_ready = sem("gram_ready")
        gram_evac = [sem(f"gram_evac{b}") for b in range(2)]
        tower_ready = sem("tower_ready")
        tower_evac = [sem(f"tower_evac{b}") for b in range(2)]
        y_stored = sem("y_stored")
        pool_gate = sem("pool_gate")

        NG = len(GROUPS)
        TRS = NL + TILES_PER_CHUNK * NG
        GR = QS // GRAM_Q
        GRS = TILES_PER_CHUNK * GR
        SPLITS = 1 + N_P

        def between(a, b):
            out, used = [], 0
            for n, step in enumerate(a):
                out.append(step)
                until = len(b) * (n + 1) // len(a)
                out += b[used:until]
                used = until
            return out + b[used:]

        FIRST_BLOCKS, BEFORE_LOOKUPS, BEFORE_ROUND, BEFORE_PAIRS, FIRST_ONEHOTS = 18, 6, 12, 24, 20

        def of(chunk, stage, *counts):
            return [(chunk, stage, *at) for at in product(*counts)]

        rows_of = lambda s: of(0, "rows", [s], range(NG))
        grams_of = lambda s: of(0, "gram", [s], range(GR))
        samples_of = lambda s: of(0, "samples", [s], range(COPIED))
        onehots_of = lambda h: of(1, "onehots", [h], range(ONEHOTS), range(KT))
        before = lambda steps: [(chunk - 1, *step) for chunk, *step in steps]
        lookups = of(1, "lookup", range(NL))
        pairs, layer1s = of(-1, "pairs", range(N_P)), of(-1, "layer1", range(M1))
        layer2s, layer3s = of(-1, "layer2", range(M2)), of(-1, "layer3", range(TILES_PER_CHUNK))
        START = (of(0, "dense vector")
                 + between(between(before(lookups[ONEHOTS:]), rows_of(0)[:3]) + between(rows_of(0)[3:], pairs[:2]),
                           before(samples_of(1)[BEFORE_ROUND:]))
                 + between(between(grams_of(0), pairs[2:] + layer1s[:3]), onehots_of(0)[:FIRST_ONEHOTS]))
        ROUND = (START
                 + between(layer1s[3:] + between(rows_of(1)[:-1], layer2s),
                           onehots_of(0)[FIRST_ONEHOTS:] + samples_of(0)[:FIRST_BLOCKS])
                 + rows_of(1)[-1:] + layer3s + of(0, "dense parts")
                 + between(grams_of(1), samples_of(0)[FIRST_BLOCKS:])
                 + samples_of(1)[:BEFORE_LOOKUPS]
                 + between(lookups[:ONEHOTS],
                           between(onehots_of(1), samples_of(1)[BEFORE_LOOKUPS:BEFORE_ROUND])))
        own = lambda steps: [(chunk + 1, *step) for chunk, *step in steps]
        LAST = (START
                + between(layer1s[3:] + between(rows_of(1)[:-1], layer2s), samples_of(0)[:FIRST_BLOCKS])
                + rows_of(1)[-1:] + layer3s + of(0, "dense parts")
                + between(grams_of(1), samples_of(0)[FIRST_BLOCKS:])
                + of(0, "layer1 step", [N_P], range(M1))
                + samples_of(1)[:BEFORE_PAIRS] + own(pairs[:1])
                + samples_of(1)[BEFORE_PAIRS:] + own(pairs[1:2])
                + of(0, "layer1 step", [0], range(2)) + own(pairs[2:]) + of(0, "layer1 step", [0], range(2, M1))
                + of(0, "layer1 step", range(1, N_P), range(M1)) + of(0, "layer1 sum", range(M1))
                + of(0, "layer2 step", range(M1), range(M2)) + of(0, "layer2 sum", range(M2)) + own(layer3s))
        FILL = []
        for n in range(ONEHOTS):
            FILL += of(1, "onehots", [0], [n], range(KT)) + of(1, "split", [n])
        for n in range(ONEHOTS):
            FILL += of(1, "lookup", [n]) + of(1, "onehots", [1], [n], range(KT)) + of(1, "split", [ONEHOTS + n])
        TR_USE = {tuple(at): n for n, at in enumerate(
            [at for ahead in (1, 0) for chunk, *at in ROUND if chunk == ahead and at[0] in ("lookup", "rows")])}
        assert len(TR_USE) == TRS and all(TR_USE["lookup", n] < TR_USE["rows", 0, NG - 1] for n in range(NL))
        AT_P = 0
        AT_1 = AT_P + N_P
        AT_2 = AT_1 + M1
        AT_3 = AT_2 + M2
        USES = AT_3 + 1
        assert USES % 2 == 0 and TRS % 2 == 0 and GRS % 2 == 0

        LOADS = [[(table_hi[:, n].rearrange("p k d -> p (k d)"), table_lo[:, n].rearrange("p k d -> p (k d)"),
                   tables[f].rearrange("(p k) d -> p (k d)", k=KT))] for n, f in enumerate(LOOKED_UP)]
        w1_sizes = [size for _, size, _ in PAIR_STEPS] + [D]
        w1_parts = [(w1_hi[0:size, c, :], w1_lo[0:size, c, :], w1[sum(w1_sizes[:c]):sum(w1_sizes[:c + 1]), :])
                    for c, size in enumerate(w1_sizes)]
        LOADS += [w1_parts[c:c + 2] for c in range(0, N_P + 1, 2)]
        LOADS += [[(w2_hi[:, c, :], w2_lo[:, c, :], w2[c * P:(c + 1) * P, :]) for c in range(M1)]]

        def staged_at(load):
            at = 0
            for hi, lo, src in LOADS[load]:
                rows_, cols = src.shape
                yield staged[load % 2][0:rows_, at:at + cols], hi, lo, src
                at += cols

        def staged_count(load):
            return 16 * sum(len(LOADS[n]) for n in range(load % 2, load + 1, 2))

        def gathered(g, chunks):
            return 16 * len(GROUPS[g]) * chunks

        def transposed(s, chunks):
            return TRS * (chunks - 1) + TR_USE["rows", s, NG - 1] + 1

        def drain_bank(m):
            return gram_ps[m // 2][:, m % 2]

        def lookup_out(n):
            return tr_ps[TR_USE["lookup", n] % 2][:, 0:TILES_PER_CHUNK, :]

        block = ctx.enter_context(nc.Block())

        @block.sync
        def _(sp):
            def load_ids_bc(h, chunk):
                sp.dma_start(ids_bc[h][:], lookup_ids[h * ONEHOTS:(h + 1) * ONEHOTS, bass.ds(chunk * NCOL, NCOL)]
                             .unsqueeze(0).to_broadcast([KP, ONEHOTS, NCOL])).then_inc(ids_bc_loaded[h], 16)

            def load_next_ids_bc(h, chunk):
                sp.wait_ge(onehot_ready[ONEHOTS - 1], 2 * chunk - 1 + h)
                load_ids_bc(h, chunk)

            def load_idx(s, i):
                t = bass.ds(i * TILES_PER_CHUNK + s, 1)
                sp.dma_start(idx[s][:], ids_v[:, t, :].rearrange("p a f -> p (a f)")).then_inc(idx_loaded[s], 16)

            def load_dense(i):
                tiles = bass.ds(i * TILES_PER_CHUNK, TILES_PER_CHUNK)
                sp.dma_start(dense_next[:].rearrange("d (t p) -> d t p", t=TILES_PER_CHUNK),
                             x_v[:, tiles, :]).then_inc(dense_loaded, 16)

            def load_tiles(i):
                for s in range(TILES_PER_CHUNK):
                    sp.wait_ge(tr_ready, transposed(s, i))
                    load_idx(s, i)
                sp.wait_ge(dense_ready, i + 1)
                load_dense(i)

            load_idx(0, 0)
            load_ids_bc(0, 0)
            for n in range(len(LOADS)):
                if n >= 2:
                    sp.wait_ge(staged_split, n - 1)
                for dst, _, _, src in staged_at(n):
                    sp.dma_start(dst, src).then_inc(staged_loaded[n % 2], 16)
                if n == 1:
                    load_idx(1, 0)
                    load_dense(0)
                    load_ids_bc(1, 0)
                if n == NL:
                    load_next_ids_bc(0, 1)
            with sp.Fori(1, CHUNKS - 1) as i:
                load_next_ids_bc(1, i)
                load_tiles(i)
                load_next_ids_bc(0, i + 1)
            load_next_ids_bc(1, CHUNKS - 1)
            load_tiles(CHUNKS - 1)
            for b in range(2):
                sp.wait_ge(tower_evac[b], CHUNKS * (USES // 2) + 1)
            sp.dma_start(y_v, y_sb[:]).then_inc(y_stored, 16)
            sp.wait_ge(y_stored, 16)

        @block.gpsimd
        def _(pool):
            pool.memset(ident[:], 0.0).then_inc(ident_zeroed, 1)
            pool.wait_ge(ident_zeroed, 1)
            pool.affine_select(out=ident[:], in_=ident[:], compare_op=ALU.not_equal, fill=1.0, base=0,
                               pattern=[[-1, P]], channel_multiplier=1).then_inc(ident_ready, 1)
            pool.iota(row_no_i[:], pattern=[[1, KT]], base=0, channel_multiplier=KT).then_inc(row_no_done, 1)

            def gather_tile(i, s, first=False):
                if not first:
                    pool.wait_ge(tr_ready, transposed(s, i))
                pool.wait_ge(idx_loaded[s], 16 * (i + 1))
                pool.sem_inc(pool_gate)
                for g, group in enumerate(GROUPS):
                    for f in group:
                        pool.indirect_dma_start(
                            out=rows[s][:, place[f], :], out_offset=None, in_=tables[f][:, :],
                            in_offset=bass.IndirectOffsetOnAxis(ap=idx[s][:, f:f + 1], axis=0),
                        ).then_inc(rows_loaded[s][g], 16)

            for s in range(TILES_PER_CHUNK):
                gather_tile(0, s, first=True)
            with pool.Fori(1, CHUNKS) as i:
                for s in range(TILES_PER_CHUNK):
                    gather_tile(i, s)

        @block.tensor
        def _(pe):
            pe.wait_ge(ident_ready, 1)

            def look_up(i, n, first=False):
                pe.wait_ge(tr_evac, TRS * i + TR_USE["lookup", n] + 1)
                pe.wait_ge(onehot_ready[n % ONEHOTS], 2 * i + n // ONEHOTS + 1)
                if first:
                    pe.wait_ge(staged_split, n + 1)
                products = [(part, k) for part in (table_hi, table_lo) for k in range(KT)]
                for part, k in products:
                    last = nc.tensor.matmul(lookup_out(n), part[:, n, k, :], onehot[:, n % ONEHOTS, k, :],
                                            start=(part, k) == products[0], stop=(part, k) == products[-1])
                last.then_inc(tr_ready, 1)

            def transpose_rows(i, s, g):
                group = GROUPS[g]
                n = TR_USE["rows", s, g]
                pe.wait_ge(rows_loaded[s][g], gathered(g, i + 1))
                pe.wait_ge(tr_evac, TRS * i + n + 1)
                for k, f in enumerate(group):
                    last = nc.tensor.transpose(tr_ps[n % 2][:, k, :], rows[s][:, place[f], :], ident[:])
                last.then_inc(tr_ready, 1)

            def gram_products(i, s, r):
                if r == 0:
                    pe.wait_ge(tr_evac, transposed(s, i + 1) + 2)
                n = s * GR + r
                pe.wait_ge(gram_evac[n % 2], 2 * (GRS // 2 * i + n // 2 + 1))
                for k in range(GRAM_Q):
                    q = r * GRAM_Q + k
                    o = gram_ps[n % 2][0:GRAM_M, k // 4, (k % 4) * PER_MM * FIELDS:(k % 4 + 1) * PER_MM * FIELDS]
                    last = nc.tensor.matmul(o, vecs[:, s, q, :, :].rearrange("p j f -> p (j f)")[:, 0:GRAM_M],
                                            vecs[:, s, q, :, 1:VECS], start=True, stop=True)
                last.then_inc(gram_ready, 1)

            def tower_bank(i, n):
                pe.wait_ge(tower_evac[n % 2], USES // 2 * i + n // 2 + 1)
                return tower_ps[n % 2]

            def tower_evacuated(i, n):
                for b in range(2):
                    pe.wait_ge(tower_evac[b], USES // 2 * i + (n + 1 - b) // 2 + 1)

            def pairs_up(i, c):
                at, size, done = PAIR_STEPS[c]
                for up in samples_up:
                    pe.wait_ge(up, COPIED * i + done + 2)
                o = tower_bank(i, AT_P + c)
                for s in range(TILES_PER_CHUNK):
                    last = nc.tensor.transpose(o[0:size, s * P:(s + 1) * P], inter[:, s, at:at + size], ident[:])
                last.then_inc(tower_ready, 1)

            def products(out, w_hi, w_lo, x_hi, x_lo, first, last):
                nc.tensor.matmul(out, w_hi, x_hi, start=first, stop=False)
                nc.tensor.matmul(out, w_hi, x_lo, start=False, stop=False)
                return nc.tensor.matmul(out, w_lo, x_hi, start=False, stop=last)

            def layer1_step(out, c, m):
                size = w1_sizes[c]
                w_hi, w_lo = (w[0:size, c, m * P:(m + 1) * P] for w in (w1_hi, w1_lo))
                x_hi, x_lo = ((pairs_hi[0:size, c, :], pairs_lo[0:size, c, :]) if c < N_P
                              else (dense_hi[:], dense_lo[:]))
                return products(out, w_hi, w_lo, x_hi, x_lo, c == N_P, c == N_P - 1)

            def layer1(i, m):
                if m == 0:
                    pe.wait_ge(dense_ready, i + 2)
                    tower_evacuated(i, AT_1)
                o = tower_bank(i, AT_1 + m)[:, 0:NCOL]
                for c in [N_P] + list(range(N_P)):
                    last = layer1_step(o, c, m)
                last.then_inc(tower_ready, 1)

            def layer2_step(out, c, m):
                w_hi, w_lo = (w[:, c, m * P:(m + 1) * P] for w in (w2_hi, w2_lo))
                return products(out, w_hi, w_lo, hid1_hi[:, c, :], hid1_lo[:, c, :], c == 0, c == M1 - 1)

            def layer2(i, m):
                if m == 0:
                    pe.wait_ge(hid1_split, M1 * (i + 1) + 2)
                o = tower_bank(i, AT_2 + m)[:, 0:NCOL]
                for c in range(M1):
                    last = layer2_step(o, c, m)
                last.then_inc(tower_ready, 1)

            def drain_layer1(i, c, m):
                if m == 0 and c == N_P:
                    pe.wait_ge(dense_ready, i + 2)
                    for b in range(2):
                        pe.wait_ge(gram_evac[b], 2 * (GRS // 2 * (i + 1) + 1))
                elif m == 0:
                    n = AT_P + c
                    pe.wait_ge(tower_evac[n % 2], USES // 2 * i + n // 2 + 2)
                last = layer1_step(drain_bank(m)[:, 0:NCOL], c, m)
                if c == N_P - 1:
                    last.then_inc(tower_ready, 1)

            def drain_layer2(i, c, m):
                if m == 0:
                    pe.wait_ge(hid1_split, M1 * i + c + 3)
                last = layer2_step(tower_ps[(AT_2 + m) % 2][:, 0:NCOL], c, m)
                if c == M1 - 1:
                    last.then_inc(tower_ready, 1)

            def layer3(i, s):
                if s == 0:
                    tower_evacuated(i, AT_3)
                o = tower_bank(i, AT_3)
                for c in range(M2):
                    last = nc.tensor.matmul(o[:, s:s + 1], hid2[:, c, s * P:(s + 1) * P], w3_sb[:, c:c + 1],
                                            start=c == 0, stop=c == M2 - 1)
                if s == TILES_PER_CHUNK - 1:
                    last.then_inc(tower_ready, 1)

            stages = {"rows": transpose_rows, "gram": gram_products, "pairs": pairs_up,
                      "layer1": layer1, "layer2": layer2, "layer3": layer3,
                      "layer1 step": drain_layer1, "layer2 step": drain_layer2}

            def take_round(i, chunks, first=False, steps=ROUND):
                for chunk, stage, *at in steps:
                    if chunk in chunks:
                        if stage == "lookup":
                            look_up(i + chunk, *at, first)
                        elif stage in stages:
                            stages[stage](i + chunk, *at)

            take_round(-1, [1], first=True, steps=FILL)
            take_round(0, [0, 1], first=True)
            pe.wait_ge(staged_split, len(LOADS))
            pe.wait_ge(weights_loaded, 16 * 3)
            with pe.Fori(1, CHUNKS - 1) as i:
                take_round(i, [-1, 0, 1])
            take_round(CHUNKS - 1, [-1, 0], steps=LAST)

        def gram_blocks(n, s, r, quads):
            for j in quads:
                quad = slice(j * SLOT, min((j + 1) * SLOT, GRAM_M))
                src = gram_ps[n % 2][quad, :, 0:4 * PER_MM * FIELDS].rearrange(
                    "p b (k j f) -> p b k j f", k=4, j=PER_MM)[:, :, :, j, :]
                yield gram[quad, :, s, r * GRAM_Q:(r + 1) * GRAM_Q].rearrange("p f (b k) -> p b k f", b=2), src

        @block.vector
        def _(dve):
            def subtract(lo, whole, hi):
                return nc.vector.tensor_tensor(lo, whole, hi.bitcast(F32), ALU.subtract)

            def split_load(i, load):
                dve.wait_ge(staged_hi, load + 1)
                for whole, hi, lo, _ in staged_at(load):
                    last = subtract(lo, whole, hi)
                last.then_inc(staged_split, 1)

            def make_onehots(i, h, o, k):
                if h == 1 and k == 0:
                    dve.wait_ge(tr_ready, TRS * i + TR_USE["lookup", o] + 1)
                if o == 0 and k == 0:
                    dve.wait_ge(ids_bc_loaded[h], 16 * (i + 1))
                made = nc.vector.tensor_scalar(onehot[:, o, k, :], ids_bc[h][:, o, :], row_no[:, k:k + 1], None,
                                               ALU.is_equal)
                if k == KT - 1:
                    made.then_inc(onehot_ready[o], 1)

            def evac_gram(i, s, r, first):
                n = s * GR + r
                dve.wait_ge(gram_ready, GRS * i + n + 1)
                if r == 0 and not first:
                    dve.wait_ge(samples_up[s], COPIED * i + 2)
                for out, src in gram_blocks(n, s, r, [0]):
                    nc.vector.tensor_copy(out, src).then_inc(gram_evac[n % 2], 1)

            def samples(i, s, step):
                if step == 0:
                    for b in range(2):
                        dve.wait_ge(gram_evac[b], 2 * (GRS // 2 * i + (s + 1) * GR // 2 + 1))
                if step == FIELDS:
                    dve.wait_ge(samples_up[s], COPIED * i + step + 2)
                    made = nc.vector.tensor_copy(inter[:, s, RUN_PAIRS[0]:RUN_PAIRS[0] + LEFT],
                                                 inter[:, s, RUN_AT[1] + P:RUN_AT[1] + P + LEFT])
                else:
                    dve.wait_ge(samples_up[s], COPIED * i + step + 1)
                    f, at = SAMPLE_STEPS[step]
                    made = nc.vector.transpose(inter[:, s, at:at + SLOT], gram[:, f - 1, s, :])
                made.then_inc(samples_up[s], 1)

            def split_dense(i):
                dve.wait_ge(hi_ready, SPLITS * i + 1)
                subtract(dense_lo[:], dense_next[:], dense_hi[:]).then_inc(dense_ready, 1)

            def split_pairs(i, c):
                n, size = AT_P + c, w1_sizes[c]
                dve.wait_ge(hi_ready, SPLITS * i + c + 2)
                subtract(pairs_lo[0:size, c, :], tower_ps[n % 2][0:size, 0:NCOL],
                         pairs_hi[0:size, c, :]).then_inc(tower_evac[n % 2], 1)

            def split_layer1(i, m):
                n = AT_1 + m
                dve.wait_ge(tower_evac[n % 2], USES // 2 * i + n // 2 + 2)
                subtract(hid1_lo[:, m, :], hid1[m % 2][:], hid1_hi[:, m, :]).then_inc(hid1_split, 1)

            stages = {"split": split_load, "onehots": make_onehots, "samples": samples,
                      "dense parts": split_dense, "pairs": split_pairs, "layer1": split_layer1,
                      "layer1 sum": split_layer1}

            def take_round(i, chunks, first=False, steps=ROUND):
                weights = iter(range(NL, len(LOADS)) if first else [])
                for chunk, stage, *at in steps:
                    if chunk in chunks:
                        if stage == "gram":
                            evac_gram(i, *at, first)
                            if (load := next(weights, None)) is not None:
                                split_load(i, load)
                        elif stage in stages:
                            stages[stage](i + chunk, *at)

            for s in range(TILES_PER_CHUNK):
                nc.vector.memset(vecs[:, s, :, :, VECS:SLOT], 0.0).then_inc(pads_ready, 1)
            dve.wait_ge(pads_ready, TILES_PER_CHUNK)
            nc.vector.memset(gram[P - SLOT:P, :, :, :], 0.0).then_inc(pads_ready, 1)
            dve.wait_ge(row_no_done, 1)
            nc.vector.tensor_copy(row_no[:], row_no_i[:]).then_inc(row_no_ready, 1)
            dve.wait_ge(row_no_ready, 1)
            for _ in range(2):
                for s in range(TILES_PER_CHUNK):
                    dve.sem_inc(samples_up[s])
                dve.sem_inc(hid1_split)
            dve.sem_inc(dense_ready)
            for b in range(2):
                dve.sem_inc(gram_evac[b])
            take_round(-1, [1], steps=FILL)
            dve.wait_ge(pads_ready, TILES_PER_CHUNK + 1)
            take_round(0, [0, 1], first=True)
            with dve.Fori(1, CHUNKS - 1) as i:
                take_round(i, [-1, 0, 1])
            take_round(CHUNKS - 1, [-1, 0], steps=LAST)

        @block.scalar
        def _(act):
            def copy(out, src):
                return nc.scalar.activation(out, src, ACT.Copy)

            def relu(out, src, bias):
                return nc.scalar.activation(out, src, ACT.Relu, bias=bias)

            def split_load(i, load):
                act.wait_ge(staged_loaded[load % 2], staged_count(load))
                for whole, hi, lo, _ in staged_at(load):
                    last = copy(hi, whole)
                last.then_inc(staged_hi, 1)

            def evac_lookup(i, n):
                act.wait_ge(tr_ready, TRS * i + TR_USE["lookup", n] + 1)
                out = vecs[:, :, :, :, LOOKED_UP[n]].rearrange("p s q j -> p s j q")
                src = lookup_out(n).rearrange("p s (j q) -> p s j q", j=PER_MM)
                copy(out, src).then_inc(tr_evac, 1)

            def evac_rows(i, s, g):
                group = GROUPS[g]
                n = TR_USE["rows", s, g]
                act.wait_ge(tr_ready, TRS * i + n + 1)
                out = vecs[:, s, :, :, group[0]:group[-1] + 1:group[1] - group[0]].rearrange("p q j f -> p f j q")
                src = tr_ps[n % 2][:, 0:len(group), :].rearrange("p f (j q) -> p f j q", j=PER_MM)
                copy(out, src).then_inc(tr_evac, 1)

            def dense_vector(i):
                act.wait_ge(dense_loaded, 16 * (i + 1))
                copy(vecs[:, :, :, :, FIELDS].rearrange("p s q j -> p s j q"),
                     dense_next[:].rearrange("p (s j q) -> p s j q", s=TILES_PER_CHUNK, j=PER_MM))

            def evac_gram(i, s, r, first):
                n = s * GR + r
                act.wait_ge(gram_ready, GRS * i + n + 1)
                if r == 0 and not first:
                    act.wait_ge(samples_up[s], COPIED * i + 2)
                for out, src in gram_blocks(n, s, r, range(1, PER_MM)):
                    last = copy(out, src)
                last.then_inc(gram_evac[n % 2], 1)

            def split_dense(i):
                copy(dense_hi[:], dense_next[:]).then_inc(hi_ready, 1)

            def split_pairs(i, c):
                n, size = AT_P + c, w1_sizes[c]
                act.wait_ge(tower_ready, USES * i + n + 1)
                copy(pairs_hi[0:size, c, :], tower_ps[n % 2][0:size, 0:NCOL]).then_inc(hi_ready, 1)

            def evac_layer1(i, m, bank=None):
                n = AT_1 + m
                src = (tower_ps[n % 2] if bank is None else bank)[:, 0:NCOL]
                act.wait_ge(tower_ready, USES * i + n + 1)
                relu(hid1_hi[:, m, :], src, b1_sb[:, m:m + 1])
                act.wait_ge(hid1_split, M1 * i + m + 1)
                relu(hid1[m % 2][:], src, b1_sb[:, m:m + 1]).then_inc(tower_evac[n % 2], 1)

            def evac_layer2(i, m):
                n = AT_2 + m
                act.wait_ge(tower_ready, USES * i + n + 1)
                relu(hid2[:, m, :], tower_ps[n % 2][:, 0:NCOL], b2_sb[:, m:m + 1]).then_inc(tower_evac[n % 2], 1)

            def evac_layer3(i, s):
                if s == TILES_PER_CHUNK - 1:
                    act.wait_ge(tower_ready, USES * i + AT_3 + 1)
                    copy(y_sb[:, bass.ds(i * TILES_PER_CHUNK, TILES_PER_CHUNK)],
                         tower_ps[AT_3 % 2][:, 0:TILES_PER_CHUNK]).then_inc(tower_evac[AT_3 % 2], 1)

            stages = {"split": split_load, "lookup": evac_lookup, "rows": evac_rows,
                      "dense vector": dense_vector, "dense parts": split_dense, "pairs": split_pairs,
                      "layer1": evac_layer1, "layer1 sum": lambda i, m: evac_layer1(i, m, drain_bank(m)),
                      "layer2": evac_layer2, "layer2 sum": evac_layer2, "layer3": evac_layer3}

            def take_round(i, chunks, first=False, steps=ROUND):
                weights = iter(range(NL, len(LOADS)) if first else [])
                for chunk, stage, *at in steps:
                    if chunk in chunks:
                        if stage == "gram":
                            evac_gram(i, *at, first)
                            if (load := next(weights, None)) is not None:
                                split_load(i, load)
                        elif stage in stages:
                            stages[stage](i + chunk, *at)

            with nc.allow_non_contiguous_dma(reason="biases and W_top3 one value per partition"):
                act.dma_start(w3_sb[:], w3.rearrange("(c p) o -> p (c o)", p=P)).then_inc(weights_loaded, 16)
                act.dma_start(b1_sb[:], b1.rearrange("(c p) -> p c", p=P)).then_inc(weights_loaded, 16)
                act.dma_start(b2_sb[:], b2.rearrange("(c p) -> p c", p=P)).then_inc(weights_loaded, 16)
            for b in range(2):
                act.sem_inc(tr_evac)
                act.sem_inc(tower_evac[b])
                act.sem_inc(gram_evac[b])
            take_round(-1, [1], steps=FILL)
            act.wait_ge(pads_ready, TILES_PER_CHUNK + 1)
            act.wait_ge(weights_loaded, 16 * 3)
            take_round(0, [0, 1], first=True)
            with act.Fori(1, CHUNKS - 1) as i:
                take_round(i, [-1, 0, 1])
            take_round(CHUNKS - 1, [-1, 0], steps=LAST)


def kernel(**inputs):
    import numpy as _np
    import concourse.bacc as _bacc
    from concourse import mybir as _mybir
    from concourse.bass_utils import run_bass_kernel_spmd as _run

    nc = _bacc.Bacc("TRN2", target_bir_lowering=False, num_devices=1)
    arrays, aps = {}, {}
    for name, a in inputs.items():
        a = _np.ascontiguousarray(a)
        arrays[f"in_{name}"] = a
        aps[name] = nc.dram_tensor(f"in_{name}", a.shape, _mybir.dt.from_np(a.dtype), kind="ExternalInput").ap()
    order = _np.ascontiguousarray(inputs["ids"]).reshape(P, -1, FIELDS)[:, :, LOOKED_UP].transpose(2, 1, 0)
    arrays["in_lookup_ids"] = _np.ascontiguousarray(order).reshape(len(LOOKED_UP), -1)
    lookup_ids = nc.dram_tensor("in_lookup_ids", arrays["in_lookup_ids"].shape, _mybir.dt.int32,
                                kind="ExternalInput").ap()
    x = _np.ascontiguousarray(inputs["r_dense_x"]).reshape(P, -1, inputs["r_dense_x"].shape[1]).transpose(2, 1, 0)
    arrays["in_x_cols"] = _np.ascontiguousarray(x).reshape(x.shape[0], -1)
    x_cols = nc.dram_tensor("in_x_cols", arrays["in_x_cols"].shape, _mybir.dt.float32, kind="ExternalInput").ap()
    first_row = [a * FIELDS - a * (a - 1) // 2 for a in range(VECS)]
    runs = [[first_row[a] + f - a - 1 for f in run for a in range(f)] for run in RUNS]
    rows = runs[0][:P] + runs[1][:P] + runs[0][P:] + runs[1][P:]
    rows += range(PAIRS, PAIRS + P)
    arrays["in_W_top1"] = _np.ascontiguousarray(inputs["W_top1"])[rows]
    y = nc.dram_tensor("out_y", (inputs["ids"].shape[0], 1), _mybir.dt.float32, kind="ExternalOutput").ap()
    dlrm_tower(nc, x_cols, aps["ids"], lookup_ids, [aps[f"tbl_{f}"] for f in range(FIELDS)],
               aps["W_top1"], aps["b_top1"], aps["W_top2"], aps["b_top2"], aps["W_top3"], y)
    return _run(nc, [arrays], core_ids=[0]).results[0]["out_y"]
```
